# Optimizing a Trainium2 kernel written in Bass

```python
import numpy as np
import jax
import jax.numpy as jnp

def _softmax(x, axis=-1):
    return jax.nn.softmax(x, axis=axis)
def _gelu(x):
    return jax.nn.gelu(x, approximate=True)
def _silu(x):
    return jax.nn.silu(x)
def _sigmoid(x):
    return jax.nn.sigmoid(x)
def _layernorm(x, axis=-1, eps=1e-5):
    m = jnp.mean(x, axis=axis, keepdims=True)
    v = jnp.var(x, axis=axis, keepdims=True)
    return (x - m) / jnp.sqrt(v + eps)
def _scatter_add(tgt, idx, src, axis=0):
    return tgt.at[idx].add(src)
def _segment_sum(src, seg, n):
    return jax.ops.segment_sum(src, seg, n)

kernel_name = 'mk_adj_preln_d1_adj_256_915fe2'

def setup_inputs(seed: int = 0):
    np.random.seed(seed)
    _w = jnp.asarray
    def _rec_inputs():
        import jax
        import jax.numpy as jnp
        _gk = jax.random.key(seed)
        x = -0.0005207 + 1.001 * jax.random.normal(jax.random.fold_in(_gk, 1), (8192, 256), jnp.float32)
        _w = (1.0 + jnp.arange(8192, dtype=jnp.float32)) ** -0.5
        _w = _w / _w.mean()
        _pij = jnp.clip(0.00195312 * _w[:, None] * _w[None, :], 0.0, 1.0)
        _a = jax.random.uniform(jax.random.fold_in(_gk, 2), (8192, 8192)) < _pij
        adj = _a.astype(jnp.int32)
        return x, adj
    x, adj = _rec_inputs()
    def _L0_gnn_setup():
        import jax, jax.numpy as jnp
        import numpy as np
        N, D = (8192, 256)
        NEG_BIG = -9000000000000000.0
        key = jax.random.key(seed)
        k1, k2, k3 = jax.random.split(key, 3)
        h = jax.random.normal(k1, (N, D), dtype=jnp.float32)
        adj = jax.random.randint(k2, (N, N), 0, 2, dtype=jnp.int32)
        bound = np.sqrt(6.0 / (2 * D + 1)).astype(np.float32)
        a = jax.random.uniform(k3, (2 * D, 1), dtype=jnp.float32, minval=-bound, maxval=bound)
        return {'h': h, 'adj': adj, 'a': a}
    _L0_gnn_all = _L0_gnn_setup()
    _L0_gnn_in = {k: v for k, v in _L0_gnn_all.items() if k in ('a', )}
    del _L0_gnn_all

    return {
        "x": x,
        "adj": adj,
        "L0_gnn_a": _L0_gnn_in["a"],
    }

def reference(x, adj, L0_gnn_a):
    import jax
    import jax.numpy as jnp
    def _L0_gnn_ref(h, adj, a):
        import jax, jax.numpy as jnp
        import numpy as np
        N, D = (8192, 256)
        NEG_BIG = -9000000000000000.0
        d = h.shape[1]
        h1 = h @ a[:d]
        h2 = h @ a[d:]
        e = jax.nn.leaky_relu(h1 + h2.T, negative_slope=0.01)
        attention = jnp.where(adj > 0, e, NEG_BIG)
        attention = jax.nn.softmax(attention, axis=1)
        return attention @ h

    h = jnp.maximum(_layernorm(x, axis=-1), 0.0)
    x = x + _L0_gnn_ref(h, adj, L0_gnn_a)
    return x


_drawn_inputs = setup_inputs


def setup_inputs(seed=0):
    import zlib

    import numpy as np

    out = dict(_drawn_inputs(seed))
    spreads = {}
    factors = {}
    for name, (base, spread) in spreads.items():
        noise = np.random.default_rng([zlib.crc32(name.encode()), seed]).standard_normal(out[name].shape)
        drawn = base * np.exp(spread * noise) if base else spread * noise
        out[name] = jnp.asarray(drawn.astype(out[name].dtype))
    for name, factor in factors.items():
        out[name] = (out[name] * factor).astype(out[name].dtype)
    return out
```

```python
import concourse.bass as bass
from concourse import mybir
from contextlib import ExitStack


def masked_graph_attention(nc, x, adj, a, out):
    f32, f32r, i32, i8 = mybir.dt.float32, mybir.dt.float32r, mybir.dt.int32, mybir.dt.int8
    f8 = mybir.dt.float8e5
    ALU = mybir.AluOpType
    ACT = mybir.ActivationFunctionType
    ds = bass.ds

    P = 128
    N, D = x.shape
    G = 4
    BLK = P * G
    NB = N // BLK
    NI = NB // 2
    NT = N // P
    CI, PI = 2, 4
    CB, PB = CI * NI, PI * NI
    NTOT = NB * NI
    PAIR = 2 * BLK
    WC = D + 2
    HL, LL = 4, 2
    PS = 128
    EPS = 1e-5
    SLOPE = 0.01
    HEADROOM = 35.0

    x_v = x.rearrange("(c p e) d -> c p (e d)", p=P, e=G)
    out_v = out.rearrange("(c p e) d -> c p (e d)", p=P, e=G)
    adj_v = adj.rearrange("(b p t) j -> b p t j", p=P, t=G)
    a_row = a.rearrange("k o -> o k")

    ctx = ExitStack()
    with ctx:
        def sb(name, shape, dt):
            return ctx.enter_context(nc.sbuf_tensor(name, shape, dt))

        def pb(name, shape, dt):
            return ctx.enter_context(nc.psum_tensor(name, shape, dt))

        def sem(name):
            return ctx.enter_context(nc.semaphore(name))

        h_hi = sb("h_hi", [P, NT, WC], f32r)
        h_lo = sb("h_lo", [P, NT, WC], f32r)
        adj_in = sb("adj_in", [P, CI, G, BLK], i32)
        mask8 = sb("mask8", [P, CI, G, BLK], f8)
        mask_words = mask8[:, :, :, :].rearrange("p c t j -> p (c t j)").bitcast(f32).rearrange(
            "p (c t w) -> p c t w", c=CI, t=G)
        E = sb("E", [P, PAIR], f32)
        W = sb("W", [P, 2, PAIR], f32)
        w_hi = sb("w_hi", [P, HL, PAIR], f32r)
        w_lo = sb("w_lo", [P, LL, PAIR], f32r)
        r_rep = sb("r_rep", [P, 2, BLK], f32)
        rb = sb("rb", [P, G, P], f32)
        ident = sb("ident", [P, P], f32)
        ones = sb("ones", [P, P], f32)
        a_rep = sb("a_rep", [P, 2 * D], f32)
        xb = sb("xb", [P, G, D], f32)
        hb = sb("hb", [P, G, D], f32)
        hsum = hb[:, 0, :]
        stage = sb("stage", [P, G, WC], f32)
        hacc = stage[:, :, 0:D]
        r_all = sb("r_all", [P, NT], f32)
        q_all = sb("q_all", [P, NT], f32)
        bst = sb("bst", [P, G, 6], f32)
        mv = sb("mv", [P, G, 2], f32)
        rstd = sb("rstd", [P, G], f32)
        mhalf = sb("mhalf", [P, G], f32)
        h12 = sb("h12", [P, 2, G], f32)
        anorm = sb("anorm", [P, 2], f32)
        nshift = sb("nshift", [P, 2], f32)
        nsum = sb("nsum", [P, 1], f32)
        floor = sb("floor", [P, 1], f32)
        eps = sb("eps", [P, G], f32)
        d_now = sb("d_now", [P, G], f32)
        half = sb("half", [P, 2], f32)
        zrow = sb("zrow", [P, G], f32)
        den = sb("den", [P, G], f32)
        rinv = sb("rinv", [P, G], f32)

        acc = pb("acc", [P, G, 512], f32)
        T = pb("T", [P, CI, BLK], f32)
        T8 = T[:, :, :].rearrange("p c w -> p (c w)").bitcast(i8).rearrange("p (c i e) -> p c e i", c=CI, e=G)
        rep = pb("rep", [P, BLK], f32)
        hs_ps = pb("hs_ps", [P, 512], f32)
        junk = hs_ps[:, :].rearrange("p (u d) -> p u d", u=2)

        s_a = sem("a_loaded")
        s_adj = [sem(f"adj_loaded{i}") for i in range(CI)]
        s_x = sem("x_loaded")
        s_const = sem("constants_ready")
        s_pool = sem("pool_step")
        s_mask = sem("mask_ready")
        s_gate = sem("convert_gate")
        s_vgate = sem("aggregate_gate")
        s_T = sem("mask_transposed")
        s_e = sem("e_ready")
        s_w = sem("w_ready")
        s_hi = sem("hi_ready")
        s_lo = sem("lo_ready")
        s_lop = sem("lo_pool_ready")
        s_used = sem("pair_used")
        s_acc = sem("acc_done")
        s_free = sem("acc_evacuated")
        s_den = sem("den_step")
        s_rinv = sem("rinv_ready")
        s_fin = sem("finish_step")
        s_o = sem("out_ready")
        s_stored = sem("out_stored")
        s_rb = sem("rb_ready")
        s_rep = sem("rep_ready")
        s_rr = sem("r_rep_ready")
        s_bn = sem("bn_done")
        s_st = sem("stats_ready")
        s_rs = sem("rstd_ready")
        s_z = sem("normed")
        s_h = sem("h_ready")
        s_dot = sem("row_sums_done")
        s_ex = sem("exps_ready")
        s_hacc = sem("hacc_done")
        s_g = sem("scaled_ready")
        s_hh = sem("h_hi_ready")
        s_hl = sem("h_lo_ready")
        s_ns = sem("nshift_ready")
        s_fl = sem("floor_ready")
        s_hp = sem("hsum_psum_ready")
        s_hs = sem("hsum_ready")

        block = ctx.enter_context(nc.Block())

        def run(eng, iteration):
            def one(b, first_block, last_block):
                iteration(b, 0, first_block, last_block, True, False)
                with eng.Fori(1, NI - 1) as it:
                    iteration(b, it, first_block, last_block, False, False)
                iteration(b, NI - 1, first_block, last_block, False, True)
            one(0, True, False)
            with eng.Fori(1, NB - 1) as b:
                one(b, False, False)
            one(NB - 1, False, True)

        @block.sync
        def _(sp):
            def load_x(c):
                sp.dma_start(xb[:, :, :].rearrange("p e d -> p (e d)"), x_v[c]).then_inc(s_x, 16)

            def load_adj(b, it, kc, wait):
                n = b * NI + it
                if wait:
                    sp.wait_ge(s_mask, n * CI + kc - 1)
                sp.dma_start(adj_in[:, kc, :, :], adj_v[b, :, :, ds((it * CI + kc) * BLK, BLK)]).then_inc(
                    s_adj[kc], 16)

            def residual(b):
                if not isinstance(b, int) or b > 0:
                    sp.wait_ge(s_stored, 16 * b)
                else:
                    sp.wait_ge(s_z, NB)
                sp.dma_start(xb[:, :, :].rearrange("p e d -> p (e d)"), x_v[b]).then_inc(s_x, 16)

            def store(b):
                sp.wait_ge(s_o, b + 1)
                sp.dma_start(out_v[b], xb[:, :, :].rearrange("p e d -> p (e d)")).then_inc(s_stored, 16)

            def iteration(b, it, first_block, last_block, first, last):
                for kc in range(CI):
                    if first_block:
                        c = it * CI + kc
                        if not (first and kc == 0):
                            sp.wait_ge(s_z, c)
                        load_x(c)
                        if first and kc == 0:
                            sp.dma_start(a_rep[:, :], a_row.partition_broadcast(P)).then_inc(s_a, 16)
                    load_adj(b, it, kc, not (first_block and first))
                if first and not first_block:
                    residual(b - 1)
                if last and not first_block:
                    store(b - 1)
            run(sp, iteration)
            residual(NB - 1)
            store(NB - 1)
            sp.wait_ge(s_stored, 16 * NB)

        @block.gpsimd
        def _(pool):
            nc.gpsimd.memset(ident[:], 0.0).then_inc(s_pool, 1)
            nc.gpsimd.memset(ones[:], 1.0)
            nc.gpsimd.memset(mhalf[:], -0.5)
            nc.gpsimd.memset(half[:], 0.5)
            nc.gpsimd.memset(eps[:], EPS)
            nc.gpsimd.memset(hacc, 0.0)
            nc.gpsimd.memset(h_hi[:, :, D + 1:WC].bitcast(f32), 0.0)
            nc.gpsimd.memset(h_lo[:, :, D + 1:WC].bitcast(f32), 0.0)
            pool.wait_ge(s_pool, 1)
            nc.gpsimd.affine_select(out=ident[:], in_=ident[:], compare_op=ALU.not_equal, fill=1.0, base=0,
                                    pattern=[[-1, P]], channel_multiplier=1).then_inc(s_const, 1)
            pool.wait_ge(s_const, 1)
            pool.wait_ge(s_dot, 2)
            nc.gpsimd.tensor_tensor(nshift[:], anorm[:], half[:], ALU.pow).then_inc(s_pool, 1)
            pool.wait_ge(s_pool, 2)
            nc.gpsimd.tensor_scalar(anorm[:], nshift[:], -(1.0 - SLOPE) * float(D) ** 0.5, HEADROOM,
                                    ALU.mult, ALU.add).then_inc(s_pool, 1)
            pool.wait_ge(s_pool, 3)
            nc.gpsimd.tensor_scalar(nshift[:], anorm[:], 0.0, None, ALU.min).then_inc(s_pool, 1)
            pool.wait_ge(s_pool, 4)
            nc.gpsimd.tensor_tensor(nsum[:], nshift[:, 0:1], nshift[:, 1:2], ALU.add).then_inc(s_ns, 1)

            def norm(c):
                pool.wait_ge(s_st, c + 1)
                if not isinstance(c, int) or c > 0:
                    pool.wait_ge(s_z, c)
                nc.gpsimd.tensor_tensor(rstd[:], mv[:, :, 1], eps[:], ALU.add).then_inc(s_pool, 1)
                pool.wait_ge(s_pool, 5 + c)
                nc.gpsimd.tensor_tensor(rstd[:], rstd[:], mhalf[:], ALU.pow).then_inc(s_rs, 1)

            def scale(c):
                pool.wait_ge(s_h, c + 1)
                nc.gpsimd.tensor_tensor(hacc, hacc, hb[:, :, :], ALU.add).then_inc(s_hacc, 1)
                pool.wait_ge(s_ex, c + 1)
                pool.wait_ge(s_hacc, c + 1)
                nc.gpsimd.tensor_tensor(hb[:, :, :], hb[:, :, :], d_now[:].unsqueeze(2).to_broadcast([P, G, D]),
                                        ALU.mult).then_inc(s_g, 1)

            def spread_r(b):
                if isinstance(b, int) and b == 0:
                    pool.wait_ge(s_ex, 1)
                else:
                    pool.wait_ge(s_rep, b)
                pool.wait_ge(s_const, 1)
                nc.gpsimd.tensor_copy(rb[:, :, :], r_all[:, ds(G * b, G)].unsqueeze(2).to_broadcast([P, G, P])
                                      ).then_inc(s_rb, 1)

            def subtract(g, k, early):
                pool.wait_ge(s_hi, g + 1)
                if not early:
                    pool.wait_ge(s_used, g + 1 - LL)
                nc.gpsimd.tensor_tensor(w_lo[:, k % LL, PAIR - PS:PAIR], W[:, k % 2, PAIR - PS:PAIR],
                                        w_hi[:, k % HL, PAIR - PS:PAIR].bitcast(f32), ALU.subtract).then_inc(s_lop, 1)

            def finish(b):
                pool.wait_ge(s_rinv, b + 1)
                pool.wait_ge(s_x, 16 * (NB + b + 1))
                if isinstance(b, int) and b == 0:
                    pool.wait_ge(s_hs, 1)
                for t in range(G):
                    u = stage[:, t, 0:D]
                    nc.gpsimd.tensor_tensor(hb[:, 1, :], hsum, zrow[:, t:t + 1].to_broadcast([P, D]), ALU.mult).then_inc(s_fin, 1)
                    pool.wait_ge(s_fin, 3 * (G * b + t) + 1)
                    nc.gpsimd.tensor_tensor(u, u, hb[:, 1, :], ALU.add).then_inc(s_fin, 1)
                    pool.wait_ge(s_fin, 3 * (G * b + t) + 2)
                    nc.gpsimd.tensor_tensor(hb[:, 2, :], u, rinv[:, t:t + 1].to_broadcast([P, D]), ALU.mult).then_inc(s_fin, 1)
                    pool.wait_ge(s_fin, 3 * (G * b + t) + 3)
                    last = nc.gpsimd.tensor_tensor(xb[:, t, :], xb[:, t, :], hb[:, 2, :], ALU.add)
                last.then_inc(s_o, 1)

            def iteration(b, it, first_block, last_block, first, last):
                n = b * NI + it
                if first and not last_block and first_block:
                    norm(0)
                    scale(0)
                    spread_r(0)
                    norm(1)
                    scale(1)
                if last and not last_block:
                    spread_r(b + 1)
                for k in range(PI):
                    if first_block and not last:
                        c = it * CI + k // 2 + 2
                        if k % 2 == 0:
                            norm(c)
                        else:
                            scale(c)
                    subtract(n * PI + k, k, first_block and first and k < LL)
                if first and not first_block:
                    finish(b - 1)

            run(pool, iteration)
            finish(NB - 1)

        @block.scalar
        def _(act):
            act.wait_ge(s_ns, 1)
            nc.scalar.activation(floor[:], nsum[:], ACT.Exp).then_inc(s_fl, 1)

            def relu(c):
                act.wait_ge(s_dot, 2 * G * (c + 1) + 2)
                hf = hb[:, :, :].rearrange("p e d -> p (e d)")
                nc.scalar.activation(hf, hf, ACT.Relu).then_inc(s_h, 1)

            def exps(c):
                k = ds(G * c, G)
                act.wait_ge(s_dot, 2 * G * (c + 1) + 2)
                nc.scalar.activation(r_all[:, k], h12[:, 0, :], ACT.Exp, bias=nshift[:, 0:1], scale=1.0 - SLOPE)
                nc.scalar.activation(q_all[:, k], h12[:, 1, :], ACT.Exp, bias=nshift[:, 1:2], scale=1.0 - SLOPE)
                nc.scalar.activation(d_now[:], h12[:, 1, :], ACT.Exp, scale=SLOPE).then_inc(s_ex, 1)

            def round_h(c):
                act.wait_ge(s_g, c + 1)
                act.wait_ge(s_ex, c + 1)
                nc.scalar.activation(h_hi[:, ds(G * c, G), 0:D], hb[:, :, :], ACT.Copy)
                nc.scalar.activation(h_hi[:, ds(G * c, G), D], d_now[:], ACT.Copy).then_inc(s_hh, 1)

            def convert(n, kc, wait):
                act.wait_ge(s_adj[kc], 16 * (n + 1))
                if wait:
                    act.wait_ge(s_T, n * CI + kc - 1)
                act.sem_inc(s_gate, 1)
                nc.scalar.activation(mask8[:, kc, :, :].rearrange("p t j -> p (t j)"),
                                     adj_in[:, kc, :, :].rearrange("p t j -> p (t j)"),
                                     ACT.Copy, bias=-0.5, scale=1.0, saturate=False).then_inc(s_mask, 1)

            def round_w(g, k, wait):
                act.wait_ge(s_w, g + 1)
                if wait:
                    act.wait_ge(s_used, g + 1 - HL)
                nc.scalar.activation(w_hi[:, k % HL, :], W[:, k % 2, :], ACT.Copy).then_inc(s_hi, 1)

            def copy_r(b):
                act.wait_ge(s_rep, b + 1)
                if not isinstance(b, int) or b > 1:
                    act.wait_ge(s_w, (b - 1) * PB)
                nc.scalar.activation(r_rep[:, b % 2, :], rep[:, :], ACT.Copy).then_inc(s_rr, 1)

            def evacuate(b):
                for t in range(G):
                    if t < G - 1:
                        act.wait_ge(s_acc, (G - 1) * b + t + 1)
                    else:
                        act.wait_ge(s_used, (b + 1) * PB)
                    if t == 0:
                        if isinstance(b, int) and b == 0:
                            act.wait_ge(s_hs, 1)
                        else:
                            act.wait_ge(s_o, b)
                    nc.scalar.activation(stage[:, t, :], acc[:, t, 0:WC], ACT.Copy).then_inc(s_free, 1)

            def iteration(b, it, first_block, last_block, first, last):
                n = b * NI + it
                if first_block and first:
                    for c in range(2):
                        exps(c)
                        relu(c)
                        if c == 0:
                            copy_r(0)
                        round_h(c)
                    convert(0, 0, False)
                for kc in range(CI):
                    if not (last_block and last and kc == 1):
                        convert(n + (kc + 1) // CI, (kc + 1) % CI, not (first_block and first and kc == 0))
                    for k in (2 * kc, 2 * kc + 1):
                        round_w(n * PI + k, k, not (first_block and first))
                        if first_block and not last:
                            c = it * CI + kc + 2
                            if k % 2 == 0:
                                exps(c)
                                relu(c)
                            else:
                                round_h(c)
                        if first and not first_block and k == 1:
                            evacuate(b - 1)
                if last and not last_block:
                    copy_r(b + 1)
                    if first_block:
                        act.wait_ge(s_hp, 1)
                        nc.scalar.activation(hsum, hs_ps[:, 0:D], ACT.Copy).then_inc(s_hs, 1)
            run(act, iteration)
            evacuate(NB - 1)

        @block.vector
        def _(dve):
            def stats(c):
                dve.wait_ge(s_x, 16 * (c + 1))
                if not isinstance(c, int) or c > 0:
                    dve.wait_ge(s_rs, c)
                for e in range(G):
                    last = nc.vector.bn_stats(bst[:, e, :], xb[:, e, :])
                last.then_inc(s_bn, 1)
                dve.wait_ge(s_bn, c + 1)
                dve.sem_inc(s_vgate, 1)
                for e in range(G):
                    last = nc.vector.bn_aggr(mv[:, e, :], bst[:, e, :])
                last.then_inc(s_st, 1)

            def normalise(c):
                dve.wait_ge(s_rs, c + 1)
                dve.wait_ge(s_st, c + 1)
                if not isinstance(c, int) or c > 0:
                    dve.wait_ge(s_hh, c)
                    dve.wait_ge(s_hl, c)
                    dve.wait_ge(s_ex, c)
                for e in range(G):
                    last = nc.vector.tensor_scalar(hb[:, e, :], xb[:, e, :], mv[:, e, 0:1], rstd[:, e:e + 1],
                                                   ALU.subtract, ALU.mult)
                last.then_inc(s_z, 1)
                dve.wait_ge(s_z, c + 1)
                for e in range(G):
                    for j in range(2):
                        dve.wait_ge(s_dot, 2 * G * c + 2 * e + j + 1)
                        nc.vector.scalar_tensor_tensor(junk[:, j, :], hb[:, e, :], 0.0, a_rep[:, j * D:(j + 1) * D],
                                                       ALU.max, ALU.mult, accum_out=h12[:, j, e:e + 1]
                                                       ).then_inc(s_dot, 1)

            def rest_h(c):
                dve.wait_ge(s_hh, c + 1)
                nc.vector.tensor_tensor(h_lo[:, ds(G * c, G), D], d_now[:],
                                        h_hi[:, ds(G * c, G), D].bitcast(f32), ALU.subtract)
                nc.vector.tensor_tensor(h_lo[:, ds(G * c, G), 0:D], hb[:, :, :],
                                        h_hi[:, ds(G * c, G), 0:D].bitcast(f32), ALU.subtract).then_inc(s_hl, 1)

            def factors(b, c, g, k):
                if not isinstance(g, int) or g > 0:
                    dve.wait_ge(s_w, g)
                for u in range(2):
                    e = 2 * (k % 2) + u
                    last = nc.vector.tensor_scalar(E[:, u * BLK:(u + 1) * BLK], r_rep[:, b % 2, :],
                                                   q_all[:, ds(G * c + e, 1)], floor[:], ALU.mult, ALU.max)
                last.then_inc(s_e, 1)

            def weights(c_tot, g, k, wait):
                dve.wait_ge(s_T, c_tot + 1)
                dve.wait_ge(s_e, g + 1)
                if wait:
                    dve.wait_ge(s_lo, g - 1)
                    dve.wait_ge(s_lop, g - 1)
                kc = k // 2
                e0 = 2 * (k % 2)
                nc.vector.scalar_tensor_tensor(W[:, k % 2, :].rearrange("p (e i) -> p e i", e=2),
                                               T8[:, kc, e0:e0 + 2, :], 0.0,
                                               E[:, :].rearrange("p (e i) -> p e i", e=2),
                                               ALU.is_gt, ALU.mult).then_inc(s_w, 1)

            def subtract(g, k, early):
                dve.wait_ge(s_hi, g + 1)
                if not early:
                    dve.wait_ge(s_used, g + 1 - LL)
                nc.vector.tensor_tensor(w_lo[:, k % LL, 0:PAIR - PS], W[:, k % 2, 0:PAIR - PS],
                                        w_hi[:, k % HL, 0:PAIR - PS].bitcast(f32), ALU.subtract).then_inc(s_lo, 1)

            def denominators(b):
                dve.wait_ge(s_free, G * (b + 1))
                if not isinstance(b, int) or b > 0:
                    dve.wait_ge(s_o, b)
                nc.vector.tensor_scalar(zrow[:], stage[:, :, D], 0.0, None, ALU.is_equal).then_inc(s_den, 1)
                dve.wait_ge(s_den, 2 * b + 1)
                nc.vector.scalar_tensor_tensor(den[:], zrow[:], float(N), stage[:, :, D],
                                               ALU.mult, ALU.add).then_inc(s_den, 1)
                dve.wait_ge(s_den, 2 * b + 2)
                nc.vector.reciprocal(rinv[:], den[:]).then_inc(s_rinv, 1)

            dve.wait_ge(s_a, 16)
            for j in range(2):
                nc.vector.scalar_tensor_tensor(junk[:, j, :], a_rep[:, j * D:(j + 1) * D], 1.0,
                                               a_rep[:, j * D:(j + 1) * D], ALU.mult, ALU.mult,
                                               accum_out=anorm[:, j:j + 1]).then_inc(s_dot, 1)
            for c in range(2):
                stats(c)
                normalise(c)
                rest_h(c)
            dve.wait_ge(s_fl, 1)

            def iteration(b, it, first_block, last_block, first, last):
                n = b * NI + it
                if first:
                    dve.wait_ge(s_rr, b + 1)
                for k in range(PI):
                    kc = k // 2
                    g = n * PI + k
                    c = it * CI + kc
                    prologue = first_block and not last
                    if prologue and k % 2 == 0:
                        stats(c + 2)
                    factors(b, c, g, k)
                    if not (first_block and first and k < 2):
                        subtract(g - 2, (k + 2) % 4, first_block and first)
                    weights(n * CI + kc, g, k, not (first_block and first and k < 2))
                    if prologue and k % 2 == 0:
                        normalise(c + 2)
                    if prologue and k % 2 == 1:
                        rest_h(c + 2)
                if first and not first_block:
                    denominators(b - 1)
            run(dve, iteration)
            for k in range(2, 4):
                subtract(NTOT * PI - 4 + k, k, False)
            denominators(NB - 1)

        @block.tensor
        def _(pe):
            pe.wait_ge(s_const, 1)

            def transpose_mask(n, kc, wait):
                g = n * CI + kc
                pe.wait_ge(s_mask, g + 1)
                if wait:
                    pe.wait_ge(s_w, 2 * (g - 1))
                for t in range(G):
                    last = nc.tensor.transpose(T[:, kc, t * P:(t + 1) * P], mask_words[:, kc, t, :], ident[:])
                last.then_inc(s_T, 1)

            def lay_out_r(b):
                pe.wait_ge(s_rb, b + 1)
                if not isinstance(b, int) or b > 0:
                    pe.wait_ge(s_rr, b)
                for t in range(G):
                    last = nc.tensor.transpose(rep[:, t * P:(t + 1) * P], rb[:, t, :], ident[:])
                last.then_inc(s_rep, 1)

            def products(b, c, g, k, start, stop, fresh):
                pe.wait_ge(s_hi, g + 1)
                pe.wait_ge(s_lo, g + 1)
                pe.wait_ge(s_lop, g + 1)
                for t in range(G):
                    if start and not fresh:
                        pe.wait_ge(s_free, G * (b - 1) + t + 1)
                    for u in range(2):
                        tile = G * c + 2 * (k % 2) + u
                        cols = slice(u * BLK + t * P, u * BLK + (t + 1) * P)
                        rhs_hi = h_hi[:, ds(tile, 1), :].rearrange("p o w -> p (o w)")
                        rhs_lo = h_lo[:, ds(tile, 1), :].rearrange("p o w -> p (o w)")
                        nc.tensor.matmul(acc[:, t, 0:WC], w_hi[:, k % HL, cols], rhs_hi,
                                         start=start and u == 0, stop=False)
                        nc.tensor.matmul(acc[:, t, 0:WC], w_hi[:, k % HL, cols], rhs_lo, start=False, stop=False)
                        last = nc.tensor.matmul(acc[:, t, 0:WC], w_lo[:, k % LL, cols], rhs_hi,
                                                start=False, stop=stop and u == 1)
                    if stop and t < G - 1:
                        last.then_inc(s_acc, 1)
                last.then_inc(s_used, 1)

            def iteration(b, it, first_block, last_block, first, last):
                n = b * NI + it
                if first_block and first:
                    lay_out_r(0)
                    transpose_mask(0, 0, False)
                    transpose_mask(0, 1, False)
                if last and not last_block:
                    lay_out_r(b + 1)
                    if first_block:
                        pe.wait_ge(s_hacc, NB)
                        for e in range(G):
                            mm = nc.tensor.matmul(hs_ps[:, 0:D], ones[:], stage[:, e, 0:D],
                                                  start=(e == 0), stop=(e == G - 1))
                        mm.then_inc(s_hp, 1)
                for k in range(PI):
                    kc = k // 2
                    c = it * CI + kc
                    if first_block:
                        pe.wait_ge(s_hl, c + 1)
                    products(b, c, n * PI + k, k, first and k == 0, last and k == PI - 1, first_block)
                    if k % 2 == 0 and not (last_block and last):
                        transpose_mask(n + 1, kc, True)
            run(pe, iteration)


_INS = ['x', 'adj', 'L0_gnn_a']


def kernel(**inputs):
    import numpy as _np
    import concourse.bacc as _bacc
    from concourse import mybir as _mybir
    from concourse.bass_utils import run_bass_kernel_spmd as _run

    nc = _bacc.Bacc("TRN2", target_bir_lowering=False, num_devices=1)
    arrays, args = {}, []
    for name in _INS:
        v = _np.ascontiguousarray(inputs[name])
        arrays[f"in_{name}_dram"] = v
        args.append(nc.dram_tensor(f"in_{name}_dram", v.shape, _mybir.dt.from_np(v.dtype), kind="ExternalInput").ap())
    shape = inputs["x"].shape
    args.append(nc.dram_tensor("out_dram", shape, _mybir.dt.from_np(_np.dtype("float32")), kind="ExternalOutput").ap())
    masked_graph_attention(nc, *args)
    r = _run(nc, [arrays], core_ids=[0])
    return r.results[0]["out_dram"]
```

```python
import concourse.bass as bass
from concourse import mybir
from contextlib import ExitStack


def masked_graph_attention(nc, x, adj, a, out):
    f32, f32r, i32, i8 = mybir.dt.float32, mybir.dt.float32r, mybir.dt.int32, mybir.dt.int8
    f8 = mybir.dt.float8e5
    ALU = mybir.AluOpType
    ACT = mybir.ActivationFunctionType
    ds = bass.ds

    P = 128
    N, D = x.shape
    G = 4
    BLK = P * G
    NB = N // BLK
    NI = NB // 2
    NT = N // P
    CI, PI = 2, 4
    CB, PB = CI * NI, PI * NI
    NTOT = NB * NI
    PAIR = 2 * BLK
    WC = D + 2
    HL, LL = 4, 2
    PS = 320
    ENDING = {0: [0, 1], 1: [2], 2: [3], 3: []}
    EPS = 1e-5
    SLOPE = 0.01
    HEADROOM = 35.0

    x_v = x.rearrange("(c p e) d -> c p (e d)", p=P, e=G)
    out_v = out.rearrange("(c p e) d -> c p (e d)", p=P, e=G)
    adj_v = adj.rearrange("(b p t) j -> b p t j", p=P, t=G)
    a_row = a.rearrange("k o -> o k")

    ctx = ExitStack()
    with ctx:
        def sb(name, shape, dt):
            return ctx.enter_context(nc.sbuf_tensor(name, shape, dt))

        def pb(name, shape, dt):
            return ctx.enter_context(nc.psum_tensor(name, shape, dt))

        def sem(name):
            return ctx.enter_context(nc.semaphore(name))

        h_hi = sb("h_hi", [P, NT, WC], f32r)
        h_lo = sb("h_lo", [P, NT, WC], f32r)
        adj_in = sb("adj_in", [P, CI, G, BLK], i32)
        mask8 = sb("mask8", [P, CI, G, BLK], f8)
        mask_words = mask8[:, :, :, :].rearrange("p c t j -> p (c t j)").bitcast(f32).rearrange(
            "p (c t w) -> p c t w", c=CI, t=G)
        E = sb("E", [P, 2, PAIR], f32)
        W = sb("W", [P, 2, PAIR], f32)
        w_hi = sb("w_hi", [P, HL, PAIR], f32r)
        w_lo = sb("w_lo", [P, LL, PAIR], f32r)
        r_rep = sb("r_rep", [P, 2, BLK], f32)
        ident = sb("ident", [P, P], f32)
        ones = sb("ones", [P, P], f32)
        a_rep = r_rep[:, 1, 0:2 * D]
        xb = sb("xb", [P, G, D], f32)
        hb = sb("hb", [P, G, D], f32)
        hmean, hshare = hb[:, 0, :], hb[:, 1, :]
        rb_later = hb[:, 2:4, :].rearrange("p a (u i) -> p (a u) i", i=P)
        rb_first = W[:, 1, 0:BLK].rearrange("p (t i) -> p t i", t=G)
        stage = sb("stage", [P, G, WC], f32)
        hacc = stage[:, :, 0:D]
        r_all = sb("r_all", [P, NT], f32)
        q_all = sb("q_all", [P, NT], f32)
        bst = sb("bst", [P, G, 6], f32)
        mv = sb("mv", [P, G, 2], f32)
        rstd = sb("rstd", [P, G], f32)
        mhalf = sb("mhalf", [P, G], f32)
        h12 = sb("h12", [P, 2, G], f32)
        anorm = sb("anorm", [P, 2], f32)
        nshift = sb("nshift", [P, 2], f32)
        nsum = sb("nsum", [P, 1], f32)
        floor = sb("floor", [P, 1], f32)
        eps = sb("eps", [P, G], f32)
        d_now = sb("d_now", [P, G], f32)
        half = sb("half", [P, 2], f32)
        zrow = sb("zrow", [P, G], f32)
        den = sb("den", [P, G], f32)
        rinv = sb("rinv", [P, G], f32)

        acc = pb("acc", [P, G, 512], f32)
        T = pb("T", [P, CI, BLK], f32)
        T8 = T[:, :, :].rearrange("p c w -> p (c w)").bitcast(i8).rearrange("p (c i e) -> p c e i", c=CI, e=G)
        rep = pb("rep", [P, BLK], f32)
        hs_ps = pb("hs_ps", [P, 512], f32)
        junk = hs_ps[:, :].rearrange("p (u d) -> p u d", u=2)

        s_a = sem("a_loaded")
        s_adj = [sem(f"adj_loaded{i}") for i in range(CI)]
        s_x = sem("x_loaded")
        s_const = sem("constants_ready")
        s_pool = sem("pool_step")
        s_mask = sem("mask_ready")
        s_gate = sem("convert_gate")
        s_vgate = sem("aggregate_gate")
        s_T = sem("mask_transposed")
        s_e = sem("e_ready")
        s_w = sem("w_ready")
        s_hi = sem("hi_ready")
        s_lo = sem("lo_ready")
        s_lop = sem("lo_pool_ready")
        s_used = sem("pair_used")
        s_acc = sem("acc_done")
        s_free = sem("acc_evacuated")
        s_den = sem("den_step")
        s_rinv = sem("rinv_ready")
        s_fin = sem("finish_step")
        s_y = sem("rows_normalised")
        s_o = sem("out_ready")
        s_stored = sem("x_buffer_free")
        s_rb = sem("rb_ready")
        s_rep = sem("rep_ready")
        s_rr = sem("r_rep_ready")
        s_bn = sem("bn_done")
        s_st = sem("stats_ready")
        s_rs = sem("rstd_ready")
        s_z = sem("normed")
        s_h = sem("h_ready")
        s_dot = sem("row_sums_done")
        s_ex = sem("exps_ready")
        s_hacc = sem("hacc_done")
        s_g = sem("scaled_ready")
        s_hh = sem("h_hi_ready")
        s_hl = sem("h_lo_ready")
        s_ns = sem("nshift_ready")
        s_fl = sem("floor_ready")
        s_hp = sem("hsum_psum_ready")
        s_hs = sem("hsum_ready")

        block = ctx.enter_context(nc.Block())

        def run(eng, iteration):
            def one(b, first_block, last_block):
                iteration(b, 0, first_block, last_block, True, False)
                with eng.Fori(1, NI - 1) as it:
                    iteration(b, it, first_block, last_block, False, False)
                iteration(b, NI - 1, first_block, last_block, False, True)
            one(0, True, False)
            with eng.Fori(1, NB - 1) as b:
                one(b, False, False)
            one(NB - 1, False, True)

        @block.sync
        def _(sp):
            def load_x(c):
                sp.dma_start(xb[:, :, :].rearrange("p e d -> p (e d)"), x_v[c]).then_inc(s_x, 16)

            def load_adj(b, it, kc, wait):
                n = b * NI + it
                if wait:
                    sp.wait_ge(s_mask, n * CI + kc - 1)
                sp.dma_start(adj_in[:, kc, :, :], adj_v[b, :, :, ds((it * CI + kc) * BLK, BLK)]).then_inc(
                    s_adj[kc], 16)

            def iteration(b, it, first_block, last_block, first, last):
                for kc in range(CI):
                    if first_block:
                        c = it * CI + kc
                        if not (first and kc == 0):
                            sp.wait_ge(s_z, c)
                        load_x(c)
                        if first and kc == 0:
                            sp.dma_start(a_rep, a_row.partition_broadcast(P)).then_inc(s_a, 16)
                    load_adj(b, it, kc, not (first_block and first))
                if last and first_block:
                    sp.wait_ge(s_z, NB)
                    sp.sem_inc(s_stored, 16)
            run(sp, iteration)
            sp.wait_ge(s_stored, 16 * (NB + 1))

        @block.gpsimd
        def _(pool):
            nc.gpsimd.memset(ident[:], 0.0).then_inc(s_pool, 1)
            nc.gpsimd.memset(ones[:], 1.0)
            nc.gpsimd.memset(mhalf[:], -0.5)
            nc.gpsimd.memset(half[:], 0.5)
            nc.gpsimd.memset(eps[:], EPS)
            nc.gpsimd.memset(hacc, 0.0)
            nc.gpsimd.memset(h_hi[:, :, D + 1:WC].bitcast(f32), 0.0)
            nc.gpsimd.memset(h_lo[:, :, D + 1:WC].bitcast(f32), 0.0)
            pool.wait_ge(s_pool, 1)
            nc.gpsimd.affine_select(out=ident[:], in_=ident[:], compare_op=ALU.not_equal, fill=1.0, base=0,
                                    pattern=[[-1, P]], channel_multiplier=1).then_inc(s_const, 1)
            pool.wait_ge(s_const, 1)
            pool.wait_ge(s_dot, 2)
            nc.gpsimd.tensor_tensor(nshift[:], anorm[:], half[:], ALU.pow).then_inc(s_pool, 1)
            pool.wait_ge(s_pool, 2)
            nc.gpsimd.tensor_scalar(anorm[:], nshift[:], -(1.0 - SLOPE) * float(D) ** 0.5, HEADROOM,
                                    ALU.mult, ALU.add).then_inc(s_pool, 1)
            pool.wait_ge(s_pool, 3)
            nc.gpsimd.tensor_scalar(nshift[:], anorm[:], 0.0, None, ALU.min).then_inc(s_pool, 1)
            pool.wait_ge(s_pool, 4)
            nc.gpsimd.tensor_tensor(nsum[:], nshift[:, 0:1], nshift[:, 1:2], ALU.add).then_inc(s_ns, 1)

            def norm(c):
                pool.wait_ge(s_st, c + 1)
                if not isinstance(c, int) or c > 0:
                    pool.wait_ge(s_z, c)
                nc.gpsimd.tensor_tensor(rstd[:], mv[:, :, 1], eps[:], ALU.add).then_inc(s_pool, 1)
                pool.wait_ge(s_pool, 5 + c)
                nc.gpsimd.tensor_tensor(rstd[:], rstd[:], mhalf[:], ALU.pow).then_inc(s_rs, 1)

            def scale(c):
                pool.wait_ge(s_h, c + 1)
                nc.gpsimd.tensor_tensor(hacc, hacc, hb[:, :, :], ALU.add).then_inc(s_hacc, 1)
                pool.wait_ge(s_ex, c + 1)
                pool.wait_ge(s_hacc, c + 1)
                nc.gpsimd.tensor_tensor(hb[:, :, :], hb[:, :, :], d_now[:].unsqueeze(2).to_broadcast([P, G, D]),
                                        ALU.mult).then_inc(s_g, 1)

            def spread_r(b):
                if isinstance(b, int) and b == 0:
                    pool.wait_ge(s_ex, 1)
                else:
                    if isinstance(b, int) and b == 1:
                        pool.wait_ge(s_hl, NB)
                    pool.wait_ge(s_rep, b)
                pool.wait_ge(s_const, 1)
                rb = rb_first if isinstance(b, int) and b == 0 else rb_later
                nc.gpsimd.tensor_copy(rb, r_all[:, ds(G * b, G)].unsqueeze(2).to_broadcast([P, G, P])
                                      ).then_inc(s_rb, 1)

            def subtract(g, k, early):
                pool.wait_ge(s_hi, g + 1)
                if not early:
                    pool.wait_ge(s_used, g + 1 - LL)
                nc.gpsimd.tensor_tensor(w_lo[:, k % LL, PAIR - PS:PAIR], W[:, k % 2, PAIR - PS:PAIR],
                                        w_hi[:, k % HL, PAIR - PS:PAIR].bitcast(f32), ALU.subtract).then_inc(s_lop, 1)

            def finish(b, t):
                i = G * b + t
                if t == 0:
                    pool.wait_ge(s_x, 16 * (NB + b + 1))
                pool.wait_ge(s_y, i + 1)
                nc.gpsimd.tensor_tensor(xb[:, t, :], xb[:, t, :], stage[:, t, 0:D], ALU.add).then_inc(s_fin, 1)
                pool.wait_ge(s_fin, i + 1)
                nc.gpsimd.tensor_tensor(xb[:, t, :], xb[:, t, :], hshare, ALU.add).then_inc(s_o, 1)

            def iteration(b, it, first_block, last_block, first, last):
                n = b * NI + it
                if first and not last_block and first_block:
                    norm(0)
                    scale(0)
                    spread_r(0)
                    norm(1)
                    scale(1)
                if (last if first_block else first) and not last_block:
                    spread_r(b + 1)
                for k in range(PI):
                    if first_block and not last:
                        c = it * CI + k // 2 + 2
                        if k % 2 == 0:
                            norm(c)
                        else:
                            scale(c)
                    subtract(n * PI + k, k, first_block and first and k < LL)
                    if last and not first_block:
                        for t in ENDING[k]:
                            finish(b - 1, t)

            run(pool, iteration)
            for t in range(G):
                finish(NB - 1, t)

        @block.scalar
        def _(act):
            act.wait_ge(s_ns, 1)
            nc.scalar.activation(floor[:], nsum[:], ACT.Exp).then_inc(s_fl, 1)

            def relu(c):
                act.wait_ge(s_dot, 2 * G * (c + 1) + 2)
                hf = hb[:, :, :].rearrange("p e d -> p (e d)")
                nc.scalar.activation(hf, hf, ACT.Relu).then_inc(s_h, 1)

            def exps(c):
                k = ds(G * c, G)
                act.wait_ge(s_dot, 2 * G * (c + 1) + 2)
                nc.scalar.activation(r_all[:, k], h12[:, 0, :], ACT.Exp, bias=nshift[:, 0:1], scale=1.0 - SLOPE)
                nc.scalar.activation(q_all[:, k], h12[:, 1, :], ACT.Exp, bias=nshift[:, 1:2], scale=1.0 - SLOPE)
                nc.scalar.activation(d_now[:], h12[:, 1, :], ACT.Exp, scale=SLOPE).then_inc(s_ex, 1)

            def round_h(c):
                act.wait_ge(s_g, c + 1)
                act.wait_ge(s_ex, c + 1)
                nc.scalar.activation(h_hi[:, ds(G * c, G), 0:D], hb[:, :, :], ACT.Copy)
                nc.scalar.activation(h_hi[:, ds(G * c, G), D], d_now[:], ACT.Copy).then_inc(s_hh, 1)

            def convert(n, kc, wait):
                act.wait_ge(s_adj[kc], 16 * (n + 1))
                if wait:
                    act.wait_ge(s_T, n * CI + kc - 1)
                act.sem_inc(s_gate, 1)
                nc.scalar.activation(mask8[:, kc, :, :].rearrange("p t j -> p (t j)"),
                                     adj_in[:, kc, :, :].rearrange("p t j -> p (t j)"),
                                     ACT.Copy, bias=-0.5, scale=1.0, saturate=False).then_inc(s_mask, 1)

            def round_w(g, k, wait):
                act.wait_ge(s_w, g + 1)
                if wait:
                    act.wait_ge(s_used, g + 1 - HL)
                nc.scalar.activation(w_hi[:, k % HL, :], W[:, k % 2, :], ACT.Copy).then_inc(s_hi, 1)

            def copy_r(b):
                if isinstance(b, int) and b == 1:
                    act.wait_ge(s_dot, 2 * G * NB + 2)
                act.wait_ge(s_rep, b + 1)
                nc.scalar.activation(r_rep[:, b % 2, :], rep[:, :], ACT.Copy).then_inc(s_rr, 1)

            def evacuate(b):
                for t in range(G):
                    if t < G - 1:
                        act.wait_ge(s_acc, (G - 1) * b + t + 1)
                    else:
                        act.wait_ge(s_used, (b + 1) * PB)
                    if t == 0:
                        if isinstance(b, int) and b == 0:
                            act.wait_ge(s_hp, 1)
                        else:
                            act.wait_ge(s_o, G * b)
                    nc.scalar.activation(stage[:, t, :], acc[:, t, 0:WC], ACT.Copy).then_inc(s_free, 1)

            def normalise(b, t):
                i = G * b + t
                if t == 0:
                    act.wait_ge(s_rinv, b + 1)
                if not isinstance(b, int) or i > 0:
                    act.wait_ge(s_o, i)
                nc.scalar.activation(stage[:, t, 0:D], stage[:, t, 0:D], ACT.Copy, scale=rinv[:, t:t + 1])
                nc.scalar.activation(hshare, hmean, ACT.Copy, scale=zrow[:, t:t + 1]).then_inc(s_y, 1)

            def load_x_again(b):
                act.wait_ge(s_stored, 16 * (b + 1))
                act.dma_start(xb[:, :, :].rearrange("p e d -> p (e d)"), x_v[b]).then_inc(s_x, 16)

            def store(b):
                act.wait_ge(s_o, G * (b + 1))
                act.dma_start(out_v[b], xb[:, :, :].rearrange("p e d -> p (e d)")).then_inc(s_stored, 16)

            def iteration(b, it, first_block, last_block, first, last):
                n = b * NI + it
                if first_block and first:
                    for c in range(2):
                        exps(c)
                        relu(c)
                        if c == 0:
                            copy_r(0)
                        round_h(c)
                    convert(0, 0, False)
                for kc in range(CI):
                    if not (last_block and last and kc == 1):
                        convert(n + (kc + 1) // CI, (kc + 1) % CI, not (first_block and first and kc == 0))
                    for k in (2 * kc, 2 * kc + 1):
                        if last and first_block and k == 1:
                            copy_r(b + 1)
                            if first_block:
                                act.wait_ge(s_hp, 1)
                                nc.scalar.activation(hmean, hs_ps[:, 0:D], ACT.Copy, scale=1.0 / N
                                                     ).then_inc(s_hs, 1)
                        round_w(n * PI + k, k, not (first_block and first))
                        if last and not first_block:
                            for t in ENDING[k]:
                                normalise(b - 1, t)
                        if first_block and not last:
                            c = it * CI + kc + 2
                            if k % 2 == 0:
                                exps(c)
                                relu(c)
                            else:
                                round_h(c)
                        if first and not first_block and k == 1:
                            evacuate(b - 1)
                if last and not first_block:
                    store(b - 1)
                if first and not first_block:
                    load_x_again(b - 1)
                    if not last_block:
                        copy_r(b + 1)
            run(act, iteration)
            evacuate(NB - 1)
            load_x_again(NB - 1)
            for t in range(G):
                normalise(NB - 1, t)
            store(NB - 1)

        @block.vector
        def _(dve):
            def stats(c):
                dve.wait_ge(s_x, 16 * (c + 1))
                if not isinstance(c, int) or c > 0:
                    dve.wait_ge(s_rs, c)
                for e in range(G):
                    last = nc.vector.bn_stats(bst[:, e, :], xb[:, e, :])
                last.then_inc(s_bn, 1)
                dve.wait_ge(s_bn, c + 1)
                dve.sem_inc(s_vgate, 1)
                for e in range(G):
                    last = nc.vector.bn_aggr(mv[:, e, :], bst[:, e, :])
                last.then_inc(s_st, 1)

            def normalise(c):
                dve.wait_ge(s_rs, c + 1)
                dve.wait_ge(s_st, c + 1)
                if not isinstance(c, int) or c > 0:
                    dve.wait_ge(s_hh, c)
                    dve.wait_ge(s_hl, c)
                    dve.wait_ge(s_ex, c)
                for e in range(G):
                    last = nc.vector.tensor_scalar(hb[:, e, :], xb[:, e, :], mv[:, e, 0:1], rstd[:, e:e + 1],
                                                   ALU.subtract, ALU.mult)
                last.then_inc(s_z, 1)
                dve.wait_ge(s_z, c + 1)
                for e in range(G):
                    for j in range(2):
                        dve.wait_ge(s_dot, 2 * G * c + 2 * e + j + 1)
                        nc.vector.scalar_tensor_tensor(junk[:, j, :], hb[:, e, :], 0.0, a_rep[:, j * D:(j + 1) * D],
                                                       ALU.max, ALU.mult, accum_out=h12[:, j, e:e + 1]
                                                       ).then_inc(s_dot, 1)

            def rest_h(c):
                dve.wait_ge(s_hh, c + 1)
                nc.vector.tensor_tensor(h_lo[:, ds(G * c, G), D], d_now[:],
                                        h_hi[:, ds(G * c, G), D].bitcast(f32), ALU.subtract)
                nc.vector.tensor_tensor(h_lo[:, ds(G * c, G), 0:D], hb[:, :, :],
                                        h_hi[:, ds(G * c, G), 0:D].bitcast(f32), ALU.subtract).then_inc(s_hl, 1)

            def factors(b, c, g, k):
                if not isinstance(g, int) or g > 1:
                    dve.wait_ge(s_w, g - 1)
                for u in range(2):
                    e = 2 * (k % 2) + u
                    last = nc.vector.tensor_scalar(E[:, k % 2, u * BLK:(u + 1) * BLK], r_rep[:, b % 2, :],
                                                   q_all[:, ds(G * c + e, 1)], floor[:], ALU.mult, ALU.max)
                last.then_inc(s_e, 1)

            def weights(c_tot, g, k, wait):
                dve.wait_ge(s_T, c_tot + 1)
                dve.wait_ge(s_e, g + 1)
                if wait:
                    dve.wait_ge(s_lo, g - 1)
                    dve.wait_ge(s_lop, g - 1)
                kc = k // 2
                e0 = 2 * (k % 2)
                nc.vector.scalar_tensor_tensor(W[:, k % 2, :].rearrange("p (e i) -> p e i", e=2),
                                               T8[:, kc, e0:e0 + 2, :], 0.0,
                                               E[:, k % 2, :].rearrange("p (e i) -> p e i", e=2),
                                               ALU.is_gt, ALU.mult).then_inc(s_w, 1)

            def subtract(g, k, early):
                dve.wait_ge(s_hi, g + 1)
                if not early:
                    dve.wait_ge(s_used, g + 1 - LL)
                nc.vector.tensor_tensor(w_lo[:, k % LL, 0:PAIR - PS], W[:, k % 2, 0:PAIR - PS],
                                        w_hi[:, k % HL, 0:PAIR - PS].bitcast(f32), ALU.subtract).then_inc(s_lo, 1)

            def denominators(b):
                dve.wait_ge(s_free, G * (b + 1))
                if not isinstance(b, int) or b > 0:
                    dve.wait_ge(s_y, G * b)
                nc.vector.tensor_scalar(zrow[:], stage[:, :, D], 0.0, None, ALU.is_equal).then_inc(s_den, 1)
                dve.wait_ge(s_den, 2 * b + 1)
                nc.vector.tensor_tensor(den[:], zrow[:], stage[:, :, D], ALU.add).then_inc(s_den, 1)
                dve.wait_ge(s_den, 2 * b + 2)
                nc.vector.reciprocal(rinv[:], den[:]).then_inc(s_rinv, 1)

            dve.wait_ge(s_a, 16)
            for j in range(2):
                nc.vector.scalar_tensor_tensor(junk[:, j, :], a_rep[:, j * D:(j + 1) * D], 1.0,
                                               a_rep[:, j * D:(j + 1) * D], ALU.mult, ALU.mult,
                                               accum_out=anorm[:, j:j + 1]).then_inc(s_dot, 1)
            for c in range(2):
                stats(c)
                normalise(c)
                rest_h(c)
            dve.wait_ge(s_fl, 1)
            dve.wait_ge(s_rr, 1)
            factors(0, 0, 0, 0)

            def iteration(b, it, first_block, last_block, first, last):
                n = b * NI + it
                for k in range(PI):
                    kc = k // 2
                    g = n * PI + k
                    c = it * CI + kc
                    prologue = first_block and not last
                    if prologue and k % 2 == 0:
                        stats(c + 2)
                    if not (first_block and first and k < 2):
                        subtract(g - 2, (k + 2) % 4, first_block and first)
                    if k < PI - 1:
                        factors(b, it * CI + (k + 1) // 2, g + 1, k + 1)
                    elif not last:
                        factors(b, it * CI + CI, g + 1, 0)
                    elif not last_block:
                        dve.wait_ge(s_rr, b + 2)
                        factors(b + 1, 0, g + 1, 0)
                    weights(n * CI + kc, g, k, not (first_block and first and k < 2))
                    if prologue and k % 2 == 0:
                        normalise(c + 2)
                    if prologue and k % 2 == 1:
                        rest_h(c + 2)
                if first and not first_block:
                    denominators(b - 1)
            run(dve, iteration)
            for k in range(2, 4):
                subtract(NTOT * PI - 4 + k, k, False)
            denominators(NB - 1)

        @block.tensor
        def _(pe):
            pe.wait_ge(s_const, 1)

            def transpose_mask(n, kc, wait):
                g = n * CI + kc
                pe.wait_ge(s_mask, g + 1)
                if wait:
                    pe.wait_ge(s_w, 2 * (g - 1))
                for t in range(G):
                    last = nc.tensor.transpose(T[:, kc, t * P:(t + 1) * P], mask_words[:, kc, t, :], ident[:])
                last.then_inc(s_T, 1)

            def lay_out_r(b):
                pe.wait_ge(s_rb, b + 1)
                if not isinstance(b, int) or b > 0:
                    pe.wait_ge(s_rr, b)
                rb = rb_first if isinstance(b, int) and b == 0 else rb_later
                for t in range(G):
                    last = nc.tensor.transpose(rep[:, t * P:(t + 1) * P], rb[:, t, :], ident[:])
                last.then_inc(s_rep, 1)

            def products(b, c, g, k, start, stop, fresh):
                pe.wait_ge(s_hi, g + 1)
                pe.wait_ge(s_lo, g + 1)
                pe.wait_ge(s_lop, g + 1)
                for t in range(G):
                    if start and not fresh:
                        pe.wait_ge(s_free, G * (b - 1) + t + 1)
                    for u in range(2):
                        tile = G * c + 2 * (k % 2) + u
                        cols = slice(u * BLK + t * P, u * BLK + (t + 1) * P)
                        rhs_hi = h_hi[:, ds(tile, 1), :].rearrange("p o w -> p (o w)")
                        rhs_lo = h_lo[:, ds(tile, 1), :].rearrange("p o w -> p (o w)")
                        nc.tensor.matmul(acc[:, t, 0:WC], w_hi[:, k % HL, cols], rhs_hi,
                                         start=start and u == 0, stop=False)
                        nc.tensor.matmul(acc[:, t, 0:WC], w_hi[:, k % HL, cols], rhs_lo, start=False, stop=False)
                        last = nc.tensor.matmul(acc[:, t, 0:WC], w_lo[:, k % LL, cols], rhs_hi,
                                                start=False, stop=stop and u == 1)
                    if stop and t < G - 1:
                        last.then_inc(s_acc, 1)
                last.then_inc(s_used, 1)

            def iteration(b, it, first_block, last_block, first, last):
                n = b * NI + it
                if first_block and first:
                    lay_out_r(0)
                    transpose_mask(0, 0, False)
                    transpose_mask(0, 1, False)
                if last and first_block:
                    lay_out_r(b + 1)
                    if first_block:
                        pe.wait_ge(s_hacc, NB)
                        for e in range(G):
                            mm = nc.tensor.matmul(hs_ps[:, 0:D], ones[:], stage[:, e, 0:D],
                                                  start=(e == 0), stop=(e == G - 1))
                        mm.then_inc(s_hp, 1)
                for k in range(PI):
                    kc = k // 2
                    c = it * CI + kc
                    if first_block:
                        pe.wait_ge(s_hl, c + 1)
                    products(b, c, n * PI + k, k, first and k == 0, last and k == PI - 1, first_block)
                    if k % 2 == 0 and not (last_block and last):
                        transpose_mask(n + 1, kc, True)
                    if k == 1 and first and not first_block and not last_block:
                        lay_out_r(b + 1)
            run(pe, iteration)


_INS = ['x', 'adj', 'L0_gnn_a']


def kernel(**inputs):
    import numpy as _np
    import concourse.bacc as _bacc
    from concourse import mybir as _mybir
    from concourse.bass_utils import run_bass_kernel_spmd as _run

    nc = _bacc.Bacc("TRN2", target_bir_lowering=False, num_devices=1)
    arrays, args = {}, []
    for name in _INS:
        v = _np.ascontiguousarray(inputs[name])
        arrays[f"in_{name}_dram"] = v
        args.append(nc.dram_tensor(f"in_{name}_dram", v.shape, _mybir.dt.from_np(v.dtype), kind="ExternalInput").ap())
    shape = inputs["x"].shape
    args.append(nc.dram_tensor("out_dram", shape, _mybir.dt.from_np(_np.dtype("float32")), kind="ExternalOutput").ap())
    masked_graph_attention(nc, *args)
    r = _run(nc, [arrays], core_ids=[0])
    return r.results[0]["out_dram"]
```

```python
import concourse.bass as bass
from concourse import mybir
from contextlib import ExitStack


def masked_graph_attention(nc, x, adj, a, out):
    f32, f32r, i32, i8 = mybir.dt.float32, mybir.dt.float32r, mybir.dt.int32, mybir.dt.int8
    f8 = mybir.dt.float8e5
    ALU = mybir.AluOpType
    ACT = mybir.ActivationFunctionType
    ds = bass.ds

    P = 128
    N, D = x.shape
    G = 4
    BLK = P * G
    NB = N // BLK
    NI = NB // 2
    NT = N // P
    CI, PI = 2, 4
    PB = PI * NI
    NTOT = NB * NI
    PAIR = 2 * BLK
    WC = D + 2
    HL, LL = 4, 2
    PS = 320
    PS0 = 768
    TAIL = 5
    EPS = 1e-5
    SLOPE = 0.01
    HEADROOM = 35.0

    x_v = x.rearrange("(c p e) d -> c p (e d)", p=P, e=G)
    x_w = x.rearrange("(c p e) d -> c p e d", p=P, e=G)
    out_w = out.rearrange("(c p e) d -> c p e d", p=P, e=G)
    out_v = out.rearrange("(c p e) d -> c p (e d)", p=P, e=G)
    adj_v = adj.rearrange("(b p t) j -> b p t j", p=P, t=G)
    a_row = a.rearrange("k o -> o k")

    ctx = ExitStack()
    with ctx:
        def sb(name, shape, dt):
            return ctx.enter_context(nc.sbuf_tensor(name, shape, dt))

        def pb(name, shape, dt):
            return ctx.enter_context(nc.psum_tensor(name, shape, dt))

        def sem(name):
            return ctx.enter_context(nc.semaphore(name))

        h_hi = sb("h_hi", [P, NT, WC], f32r)
        h_lo = sb("h_lo", [P, NT, D], f32r)
        adj_in = sb("adj_in", [P, CI, G, BLK], i32)
        mask8 = sb("mask8", [P, CI, G, BLK], f8)
        x_last = adj_in[:, 0, 0:2, :].rearrange("p u j -> p (u j)").bitcast(f32).rearrange("p (e d) -> p e d", e=G)
        mask_words = mask8[:, :, :, :].rearrange("p c t j -> p (c t j)").bitcast(f32).rearrange(
            "p (c t w) -> p c t w", c=CI, t=G)
        E = sb("E", [P, 2, PAIR], f32)
        W = sb("W", [P, 2, PAIR], f32)
        w_hi = sb("w_hi", [P, HL, PAIR], f32r)
        w_lo = sb("w_lo", [P, LL, PAIR], f32r)
        r_rep = sb("r_rep", [P, 2, BLK], f32)
        ident = sb("ident", [P, P], f32)
        ones = sb("ones", [P, P], f32r)
        a_rep = r_rep[:, 1, 0:2 * D]
        xb = sb("xb", [P, G, D], f32)
        hb = sb("hb", [P, G, D], f32)
        hmean, hshare = hb[:, 0, :], hb[:, 1, :]
        stage = sb("stage", [P, G, WC], f32)
        x_bufs = [xb[:, :, :], stage[:, :, 0:D]]
        h_bufs = [hb[:, :, :], stage[:, :, 0:D]]
        r_all = sb("r_all", [P, NT], f32)
        r_next = sb("r_next", [P, G], f32)
        q_all = sb("q_all", [P, NT], f32)
        f_all = sb("f_all", [P, NT], f32)
        bst = sb("bst", [P, CI, G, 6], f32)
        mv = sb("mv", [P, CI, G, 2], f32)
        rstd = sb("rstd", [P, CI, G], f32)
        nmean = sb("nmean", [P, G], f32)
        shift = sb("shift", [P, CI, G], f32)
        zeros = sb("zeros", [P, G], f32)
        mhalf = sb("mhalf", [P, G], f32)
        h12 = sb("h12", [P, CI, 2, G], f32)
        anorm = sb("anorm", [P, 2], f32)
        nshift = sb("nshift", [P, 2], f32)
        nsum = sb("nsum", [P, 1], f32)
        eps = sb("eps", [P, G], f32)
        half = sb("half", [P, 2], f32)
        zrow = sb("zrow", [P, G], f32)
        den = sb("den", [P, G], f32)
        rinv = sb("rinv", [P, G], f32)

        acc = pb("acc", [P, G, 512], f32)
        T = pb("T", [P, CI, BLK], f32)
        T8 = T[:, :, :].rearrange("p c w -> p (c w)").bitcast(i8).rearrange("p (c i e) -> p c e i", c=CI, e=G)
        rep = pb("rep", [P, BLK], f32)
        hs_ps = pb("hs_ps", [P, 512], f32)
        head_junk = hs_ps[:, :].rearrange("p (u d) -> p u d", u=2)
        junk = rep[:, :].rearrange("p (u d) -> p u d", u=2)

        s_a = sem("a_loaded")
        s_adj = [sem(f"adj_loaded{i}") for i in range(CI)]
        s_x = [sem("x_even_loaded"), sem("x_odd_loaded")]
        s_xlast = sem("x_of_last_block_loaded")
        s_tail = sem("last_block_step")
        s_rb = sem("r_picked")
        s_const = sem("constants_ready")
        s_pool = sem("pool_step")
        s_mask = sem("mask_ready")
        s_gate = sem("convert_gate")
        s_vgate = sem("aggregate_gate")
        s_T = sem("mask_transposed")
        s_e = sem("e_ready")
        s_w = sem("w_ready")
        s_hi = sem("hi_ready")
        s_lo = sem("lo_ready")
        s_lop = sem("lo_pool_ready")
        s_used = sem("pair_used")
        s_acc = sem("acc_done")
        s_free = sem("acc_evacuated")
        s_den = sem("den_step")
        s_rinv = sem("rinv_ready")
        s_fin = sem("finish_step")
        s_y = sem("rows_normalised")
        s_o = sem("out_ready")
        s_stored = sem("x_buffer_free")
        s_rep = sem("rep_ready")
        s_rr = sem("r_rep_ready")
        s_bn = sem("bn_done")
        s_st = sem("stats_ready")
        s_rs = sem("rstd_ready")
        s_z = sem("normed")
        s_dot = sem("row_sums_done")
        s_ex = sem("exps_ready")
        s_hsum = sem("h_summed")
        s_hh = sem("h_hi_ready")
        s_hl = sem("h_lo_ready")
        s_ns = sem("nshift_ready")
        s_mean = sem("h_mean_ready")

        block = ctx.enter_context(nc.Block())

        def run(eng, iteration):
            def one(b, first_block, last_block):
                iteration(b, 0, first_block, last_block, True, False)
                with eng.Fori(1, NI - 1) as it:
                    iteration(b, it, first_block, last_block, False, False)
                iteration(b, NI - 1, first_block, last_block, False, True)
            one(0, True, False)
            with eng.Fori(1, NB - 1) as b:
                one(b, False, False)
            one(NB - 1, False, True)

        @block.sync
        def _(sp):
            def load_x(c, parity, wait):
                if wait and parity == 0:
                    sp.wait_ge(s_z, c - 1)
                elif wait:
                    sp.wait_ge(s_hl, c - 1)
                    sp.wait_ge(s_dot, 2 * G * (c - 1) + 2)
                sp.dma_start(x_bufs[parity], x_w[c]).then_inc(s_x[parity], 16)

            def load_adj(b, it, kc, wait):
                n = b * NI + it
                if wait:
                    sp.wait_ge(s_mask, n * CI + kc - 1)
                sp.dma_start(adj_in[:, kc, :, :], adj_v[b, :, :, ds((it * CI + kc) * BLK, BLK)]).then_inc(
                    s_adj[kc], 16)

            def iteration(b, it, first_block, last_block, first, last):
                if first_block and first:
                    load_x(0, 0, False)
                    sp.dma_start(a_rep, a_row.partition_broadcast(P)).then_inc(s_a, 16)
                    load_x(1, 1, False)
                for kc in range(CI):
                    if first_block and not first:
                        load_x(it * CI + kc, kc, True)
                    load_adj(b, it, kc, not (first_block and first))
                if last and first_block:
                    sp.wait_ge(s_z, NB)
                    sp.sem_inc(s_stored, 16)
            run(sp, iteration)
            sp.wait_ge(s_mask, NTOT * CI - 1)
            sp.dma_start(x_last, x_w[NB - 1]).then_inc(s_xlast, 16)
            for t in range(G):
                sp.wait_ge(s_tail, TAIL * (t + 1))
                sp.dma_start(out_w[NB - 1][:, t, :], x_last[:, t, :]).then_inc(s_stored, 16)
            sp.wait_ge(s_stored, 16 * (NB + G))

        @block.gpsimd
        def _(pool):
            nc.gpsimd.memset(ident[:], 0.0).then_inc(s_pool, 1)
            nc.gpsimd.memset(ones[:].bitcast(f32), 1.0)
            nc.gpsimd.memset(mhalf[:], -0.5)
            nc.gpsimd.memset(half[:], 0.5)
            nc.gpsimd.memset(eps[:], EPS)
            nc.gpsimd.memset(zeros[:], 0.0)
            nc.gpsimd.memset(h_hi[:, :, D:D + 1].bitcast(f32), 1.0)
            nc.gpsimd.memset(h_hi[:, :, D + 1:WC].bitcast(f32), 0.0)
            pool.wait_ge(s_pool, 1)
            nc.gpsimd.affine_select(out=ident[:], in_=ident[:], compare_op=ALU.not_equal, fill=1.0, base=0,
                                    pattern=[[-1, P]], channel_multiplier=1).then_inc(s_const, 1)
            pool.wait_ge(s_const, 1)
            pool.wait_ge(s_dot, 2)
            nc.gpsimd.tensor_tensor(nshift[:], anorm[:], half[:], ALU.pow).then_inc(s_pool, 1)
            pool.wait_ge(s_pool, 2)
            nc.gpsimd.tensor_scalar(anorm[:], nshift[:], -float(D) ** 0.5, HEADROOM,
                                    ALU.mult, ALU.add).then_inc(s_pool, 1)
            pool.wait_ge(s_pool, 3)
            nc.gpsimd.tensor_scalar(nshift[:], anorm[:], 0.0, None, ALU.min).then_inc(s_pool, 1)
            pool.wait_ge(s_pool, 4)
            nc.gpsimd.tensor_tensor(nsum[:], nshift[:, 0:1], nshift[:, 1:2], ALU.add).then_inc(s_ns, 1)

            def norm(c, parity):
                pool.wait_ge(s_st, c + 1)
                if not isinstance(c, int) or c > 1:
                    pool.wait_ge(s_z, c - 1)
                nc.gpsimd.tensor_tensor(rstd[:, parity, :], mv[:, parity, :, 1], eps[:], ALU.add).then_inc(s_pool, 1)
                if not isinstance(c, int) or c > 0:
                    pool.wait_ge(s_rs, c)
                nc.gpsimd.tensor_tensor(nmean[:], zeros[:], mv[:, parity, :, 0], ALU.subtract)
                pool.wait_ge(s_pool, 2 * c + 5)
                nc.gpsimd.tensor_tensor(rstd[:, parity, :], rstd[:, parity, :], mhalf[:], ALU.pow).then_inc(s_pool, 1)
                pool.wait_ge(s_pool, 2 * c + 6)
                nc.gpsimd.tensor_tensor(shift[:, parity, :], nmean[:], rstd[:, parity, :], ALU.mult).then_inc(s_rs, 1)

            def rest_h(c, parity):
                h = h_bufs[parity]
                pool.wait_ge(s_hh, c + 1)
                tiles = ds(G * c, G)
                nc.gpsimd.tensor_tensor(h_lo[:, tiles, 0:D], h[:, :, :], h_hi[:, tiles, 0:D].bitcast(f32),
                                        ALU.subtract).then_inc(s_hl, 1)

            def pick_r(b):
                if isinstance(b, int) and b == 1:
                    pool.wait_ge(s_ex, 2)
                else:
                    pool.wait_ge(s_rep, b)
                pool.wait_ge(s_const, 1)
                nc.gpsimd.tensor_copy(r_next[:], r_all[:, ds(G * b, G)]).then_inc(s_rb, 1)

            def subtract(g, k, early, ps):
                pool.wait_ge(s_hi, g + 1)
                if not early:
                    pool.wait_ge(s_used, g + 1 - LL)
                nc.gpsimd.tensor_tensor(w_lo[:, k % LL, PAIR - ps:PAIR], W[:, k % 2, PAIR - ps:PAIR],
                                        w_hi[:, k % HL, PAIR - ps:PAIR].bitcast(f32), ALU.subtract).then_inc(s_lop, 1)

            def finish(b, t):
                i = G * b + t
                if t == 0:
                    pool.wait_ge(s_x[0], 16 * (NB // 2 + b + 1))
                pool.wait_ge(s_y, i + 1)
                nc.gpsimd.tensor_tensor(xb[:, t, :], xb[:, t, :], stage[:, t, 0:D], ALU.add).then_inc(s_fin, 1)
                pool.wait_ge(s_fin, i + 1)
                nc.gpsimd.tensor_tensor(xb[:, t, :], xb[:, t, :], hshare, ALU.add).then_inc(s_o, 1)

            def iteration(b, it, first_block, last_block, first, last):
                n = b * NI + it
                if first_block and first:
                    norm(0, 0)
                    norm(1, 1)
                    rest_h(0, 0)
                if (last if first_block else first) and not last_block:
                    pick_r(b + 1)
                for k in range(PI):
                    if first_block and not last:
                        c = it * CI + k // 2 + 2
                        if k % 2 == 0:
                            norm(c, k // 2)
                        else:
                            if first and k == 1:
                                rest_h(1, 1)
                            rest_h(c, k // 2)
                    subtract(n * PI + k, k, first_block and first and k < LL,
                             PS0 if first_block and not (last and k >= 2) else PS)
                    if first and not first_block and k == 3:
                        finish(b - 1, 0)
                    if last and not first_block and k < 3:
                        finish(b - 1, k + 1)
            run(pool, iteration)

        @block.scalar
        def _(act):
            def h_rows(c, parity):
                h = h_bufs[parity]
                xs = x_bufs[parity]
                act.wait_ge(s_rs, c + 1)
                if not isinstance(c, int) or c > 1:
                    act.wait_ge(s_hl, c - 1)
                for e in range(G):
                    last = nc.scalar.activation(h[:, e, :], xs[:, e, :], ACT.Relu, bias=shift[:, parity, e:e + 1],
                                                scale=rstd[:, parity, e:e + 1])
                last.then_inc(s_z, 1)

            def exps(c, parity):
                k = ds(G * c, G)
                act.wait_ge(s_dot, 2 * G * (c + 1) + 2)
                if isinstance(c, int) and c == 0:
                    act.wait_ge(s_ns, 1)
                nc.scalar.activation(r_all[:, k], h12[:, parity, 0, :], ACT.Exp, bias=nshift[:, 0:1], scale=1.0 - SLOPE)
                nc.scalar.activation(f_all[:, k], h12[:, parity, 1, :], ACT.Exp, bias=nsum[:], scale=SLOPE)
                nc.scalar.activation(q_all[:, k], h12[:, parity, 1, :], ACT.Exp, bias=nshift[:, 1:2]).then_inc(s_ex, 1)

            def round_h(c, parity):
                h = h_bufs[parity]
                act.wait_ge(s_z, c + 1)
                nc.scalar.activation(h_hi[:, ds(G * c, G), 0:D], h[:, :, :], ACT.Copy).then_inc(s_hh, 1)

            def convert(n, kc, wait):
                act.wait_ge(s_adj[kc], 16 * (n + 1))
                if wait:
                    act.wait_ge(s_T, n * CI + kc - 1)
                act.sem_inc(s_gate, 1)
                nc.scalar.activation(mask8[:, kc, :, :].rearrange("p t j -> p (t j)"),
                                     adj_in[:, kc, :, :].rearrange("p t j -> p (t j)"),
                                     ACT.Copy, bias=-0.5, scale=1.0, saturate=False).then_inc(s_mask, 1)

            def round_w(g, k, wait):
                act.wait_ge(s_w, g + 1)
                if wait:
                    act.wait_ge(s_used, g + 1 - HL)
                nc.scalar.activation(w_hi[:, k % HL, :], W[:, k % 2, :], ACT.Copy).then_inc(s_hi, 1)

            def copy_r(b):
                if isinstance(b, int) and b == 1:
                    act.wait_ge(s_dot, 2 * G * NB + 2)
                act.wait_ge(s_rep, b + 1)
                nc.scalar.activation(r_rep[:, b % 2, :], rep[:, :], ACT.Copy).then_inc(s_rr, 1)

            def evacuate(b, rows):
                for t in rows:
                    if t < G - 1:
                        act.wait_ge(s_acc, (G - 1) * b + t + 1)
                    else:
                        act.wait_ge(s_used, (b + 1) * PB)
                    if t == 0:
                        if not isinstance(b, int) or b > 0:
                            act.wait_ge(s_o, G * b)
                    nc.scalar.activation(stage[:, t, :], acc[:, t, 0:WC], ACT.Copy).then_inc(s_free, 1)

            def normalise(b, t):
                i = G * b + t
                if t == 0:
                    act.wait_ge(s_rinv, b + 1)
                if not isinstance(b, int) or i > 0:
                    act.wait_ge(s_o, i)
                nc.scalar.activation(stage[:, t, 0:D], stage[:, t, 0:D], ACT.Copy, scale=rinv[:, t:t + 1])
                nc.scalar.activation(hshare, hmean, ACT.Copy, scale=zrow[:, t:t + 1]).then_inc(s_y, 1)

            def load_x_again(b):
                act.wait_ge(s_stored, 16 * (b + 1))
                act.dma_start(xb[:, :, :].rearrange("p e d -> p (e d)"), x_v[b]).then_inc(s_x[0], 16)

            def store(b):
                act.wait_ge(s_o, G * (b + 1))
                act.dma_start(out_v[b], xb[:, :, :].rearrange("p e d -> p (e d)")).then_inc(s_stored, 16)

            def iteration(b, it, first_block, last_block, first, last):
                n = b * NI + it
                if first_block and first:
                    h_rows(0, 0)
                    h_rows(1, 1)
                    exps(0, 0)
                    convert(0, 0, False)
                    copy_r(0)
                    round_h(0, 0)
                    round_h(1, 1)
                    exps(1, 1)
                for kc in range(CI):
                    if not (last_block and last and kc == 1):
                        convert(n + (kc + 1) // CI, (kc + 1) % CI, not (first_block and first and kc == 0))
                    if first and not first_block and kc == 1:
                        evacuate(b - 1, range(2, G))
                    for k in (2 * kc, 2 * kc + 1):
                        if first_block and k % 2 == 0 and not (first and k == 0) and not (last and k == 2):
                            exps(it * CI + kc + 1, (kc + 1) % CI)
                        round_w(n * PI + k, k, not (first_block and first))
                        if last and first_block and k == 1:
                            copy_r(b + 1)
                        if first and not first_block and k == 3:
                            normalise(b - 1, 0)
                        if last and not first_block and k < 3:
                            normalise(b - 1, k + 1)
                        if first_block and not last and k % 2 == 0:
                            h_rows(it * CI + kc + 2, kc)
                            round_h(it * CI + kc + 2, kc)
                        if first and not first_block and k == 1:
                            evacuate(b - 1, range(0, 2))
                        if first and not first_block and k == 2:
                            load_x_again(b - 1)
                if last and first_block:
                    act.wait_ge(s_hsum, NB)
                    act.wait_ge(s_hl, NB)
                    nc.scalar.activation(hmean, hs_ps[:, 0:D], ACT.Copy, scale=1.0 / N).then_inc(s_mean, 1)
                if last and not first_block:
                    store(b - 1)
                if first and not first_block and not last_block:
                    copy_r(b + 1)
            run(act, iteration)

        @block.vector
        def _(dve):
            def stats(pair, parity):
                c = 2 * pair + parity
                xs = x_bufs[parity]
                dve.wait_ge(s_x[parity], 16 * (pair + 1))
                if not isinstance(c, int) or c > 1:
                    dve.wait_ge(s_rs, c - 1)
                for e in range(G):
                    last = nc.vector.bn_stats(bst[:, parity, e, :], xs[:, e, :])
                last.then_inc(s_bn, 1)
                dve.wait_ge(s_bn, c + 1)
                dve.sem_inc(s_vgate, 1)
                for e in range(G):
                    last = nc.vector.bn_aggr(mv[:, parity, e, :], bst[:, parity, e, :])
                last.then_inc(s_st, 1)

            def scores(c, parity):
                h = h_bufs[parity]
                dve.wait_ge(s_z, c + 1)
                if not isinstance(c, int) or c > 1:
                    dve.wait_ge(s_ex, c - 1)
                out = head_junk if isinstance(c, int) and c < 2 else junk
                for e in range(G):
                    for j in range(2):
                        dve.wait_ge(s_dot, 2 * G * c + 2 * e + j + 1)
                        nc.vector.scalar_tensor_tensor(out[:, j, :], h[:, e, :], 1.0, a_rep[:, j * D:(j + 1) * D],
                                                       ALU.mult, ALU.mult, accum_out=h12[:, parity, j, e:e + 1]
                                                       ).then_inc(s_dot, 1)

            def factors(b, c, g, k):
                if not isinstance(g, int) or g > 1:
                    dve.wait_ge(s_w, g - 1)
                for u in range(2):
                    e = 2 * (k % 2) + u
                    last = nc.vector.tensor_scalar(E[:, k % 2, u * BLK:(u + 1) * BLK], r_rep[:, b % 2, :],
                                                   q_all[:, ds(G * c + e, 1)], f_all[:, ds(G * c + e, 1)],
                                                   ALU.mult, ALU.max)
                last.then_inc(s_e, 1)

            def weights(c_tot, g, k, wait):
                dve.wait_ge(s_T, c_tot + 1)
                dve.wait_ge(s_e, g + 1)
                if wait:
                    dve.wait_ge(s_lo, g - 1)
                    dve.wait_ge(s_lop, g - 1)
                kc = k // 2
                e0 = 2 * (k % 2)
                nc.vector.scalar_tensor_tensor(W[:, k % 2, :].rearrange("p (e i) -> p e i", e=2),
                                               T8[:, kc, e0:e0 + 2, :], 0.0,
                                               E[:, k % 2, :].rearrange("p (e i) -> p e i", e=2),
                                               ALU.is_gt, ALU.mult).then_inc(s_w, 1)

            def subtract(g, k, early, ps):
                dve.wait_ge(s_hi, g + 1)
                if not early:
                    dve.wait_ge(s_used, g + 1 - LL)
                nc.vector.tensor_tensor(w_lo[:, k % LL, 0:PAIR - ps], W[:, k % 2, 0:PAIR - ps],
                                        w_hi[:, k % HL, 0:PAIR - ps].bitcast(f32), ALU.subtract).then_inc(s_lo, 1)

            def denominators(b):
                dve.wait_ge(s_free, G * (b + 1))
                if not isinstance(b, int) or b > 0:
                    dve.wait_ge(s_y, G * b)
                nc.vector.tensor_scalar(zrow[:], stage[:, :, D], 0.0, None, ALU.is_equal).then_inc(s_den, 1)
                dve.wait_ge(s_den, 2 * b + 1)
                nc.vector.tensor_tensor(den[:], zrow[:], stage[:, :, D], ALU.add).then_inc(s_den, 1)
                dve.wait_ge(s_den, 2 * b + 2)
                nc.vector.reciprocal(rinv[:], den[:]).then_inc(s_rinv, 1)

            dve.wait_ge(s_a, 16)
            for j in range(2):
                nc.vector.scalar_tensor_tensor(head_junk[:, j, :], a_rep[:, j * D:(j + 1) * D], 1.0,
                                               a_rep[:, j * D:(j + 1) * D], ALU.mult, ALU.mult,
                                               accum_out=anorm[:, j:j + 1]).then_inc(s_dot, 1)
            stats(0, 0)
            stats(0, 1)
            scores(0, 0)
            scores(1, 1)
            stats(1, 0)
            dve.wait_ge(s_rr, 1)
            factors(0, 0, 0, 0)
            weights(0, 0, 0, False)

            def iteration(b, it, first_block, last_block, first, last):
                n = b * NI + it
                for k in range(PI):
                    kc = k // 2
                    g = n * PI + k
                    c = it * CI + kc
                    if not (first_block and first and k < 2):
                        subtract(g - 2, (k + 2) % 4, first_block and first, PS0 if first_block else PS)
                    if first_block and (k == 1 or k == 3 and not last):
                        dve.wait_ge(s_ex, c + 2)
                    if k < PI - 1:
                        factors(b, it * CI + (k + 1) // 2, g + 1, k + 1)
                    elif not last:
                        factors(b, it * CI + CI, g + 1, 0)
                    elif not last_block:
                        dve.wait_ge(s_rr, b + 2)
                        factors(b + 1, 0, g + 1, 0)
                    if first_block and k % 2 == 0 and not (first and k == 0):
                        if not (last and k == 2):
                            scores(c + 1, (kc + 1) % 2)
                        if not last:
                            stats(it + 1, kc)
                    if first and not first_block and k == 3:
                        denominators(b - 1)
                    if not (first_block and first and k == 0):
                        weights(n * CI + kc, g, k, not (first_block and first and k < 2))
            run(dve, iteration)
            for k in range(2, 4):
                subtract(NTOT * PI - 4 + k, k, False, PS)
            dve.wait_ge(s_xlast, 16)
            dve.wait_ge(s_mean, 1)
            dve.wait_ge(s_y, G * (NB - 1))
            for t in range(G):
                if t < G - 1:
                    dve.wait_ge(s_acc, (G - 1) * (NB - 1) + t + 1)
                else:
                    dve.wait_ge(s_used, NB * PB)
                col = slice(t, t + 1)
                nc.vector.tensor_scalar(zrow[:, col], acc[:, t, D:D + 1], 0.0, None, ALU.is_equal).then_inc(s_tail, 1)
                dve.wait_ge(s_tail, TAIL * t + 1)
                nc.vector.tensor_tensor(den[:, col], zrow[:, col], acc[:, t, D:D + 1], ALU.add).then_inc(s_tail, 1)
                nc.vector.scalar_tensor_tensor(x_last[:, t, :], hmean, zrow[:, col], x_last[:, t, :],
                                               ALU.mult, ALU.add).then_inc(s_tail, 1)
                dve.wait_ge(s_tail, TAIL * t + 3)
                nc.vector.reciprocal(rinv[:, col], den[:, col]).then_inc(s_tail, 1)
                dve.wait_ge(s_tail, TAIL * t + 4)
                nc.vector.scalar_tensor_tensor(x_last[:, t, :], acc[:, t, 0:D], rinv[:, col], x_last[:, t, :],
                                               ALU.mult, ALU.add).then_inc(s_tail, 1)

        @block.tensor
        def _(pe):
            pe.wait_ge(s_const, 1)

            def transpose_mask(n, kc, wait):
                g = n * CI + kc
                pe.wait_ge(s_mask, g + 1)
                if wait:
                    pe.wait_ge(s_w, 2 * (g - 1))
                for t in range(G):
                    last = nc.tensor.transpose(T[:, kc, t * P:(t + 1) * P], mask_words[:, kc, t, :], ident[:])
                last.then_inc(s_T, 1)

            def lay_out_r(b):
                if isinstance(b, int) and b == 0:
                    pe.wait_ge(s_ex, 1)
                    r = r_all
                else:
                    pe.wait_ge(s_rb, b)
                    if isinstance(b, int) and b == 1:
                        pe.wait_ge(s_dot, 2 * G * NB + 2)
                    pe.wait_ge(s_rr, b)
                    r = r_next
                for t in range(G):
                    last = nc.tensor.transpose(rep[:, t * P:(t + 1) * P], r[:, t:t + 1].to_broadcast([P, P]),
                                               ident[:])
                last.then_inc(s_rep, 1)

            def sum_h(c, start, stop):
                if isinstance(c, int) and c == 0:
                    pe.wait_ge(s_dot, 4 * G + 2)
                for e in range(G):
                    for part, h in enumerate((h_hi, h_lo)):
                        last = nc.tensor.matmul(hs_ps[:, 0:D], ones[:],
                                                h[:, ds(G * c + e, 1), 0:D].rearrange("p o d -> p (o d)"),
                                                start=start and e == 0 and part == 0,
                                                stop=stop and e == G - 1 and part == 1, skip_group_check=True)
                last.then_inc(s_hsum, 1)

            def products(b, c, g, k, start, stop, fresh):
                pe.wait_ge(s_hi, g + 1)
                pe.wait_ge(s_lo, g + 1)
                pe.wait_ge(s_lop, g + 1)
                for t in range(G):
                    if start and not fresh:
                        pe.wait_ge(s_free, G * (b - 1) + t + 1)
                    for u in range(2):
                        tile = G * c + 2 * (k % 2) + u
                        cols = slice(u * BLK + t * P, u * BLK + (t + 1) * P)
                        rhs_hi = h_hi[:, ds(tile, 1), :].rearrange("p o w -> p (o w)")
                        rhs_lo = h_lo[:, ds(tile, 1), :].rearrange("p o w -> p (o w)")
                        nc.tensor.matmul(acc[:, t, 0:WC], w_hi[:, k % HL, cols], rhs_hi,
                                         start=start and u == 0, stop=False)
                        nc.tensor.matmul(acc[:, t, 0:D], w_hi[:, k % HL, cols], rhs_lo, start=False, stop=False)
                        last = nc.tensor.matmul(acc[:, t, 0:WC], w_lo[:, k % LL, cols], rhs_hi,
                                                start=False, stop=stop and u == 1)
                    if stop and t < G - 1:
                        last.then_inc(s_acc, 1)
                last.then_inc(s_used, 1)

            def iteration(b, it, first_block, last_block, first, last):
                n = b * NI + it
                if first_block and first:
                    lay_out_r(0)
                    transpose_mask(0, 0, False)
                    transpose_mask(0, 1, False)
                if last and first_block:
                    lay_out_r(b + 1)
                for k in range(PI):
                    kc = k // 2
                    c = it * CI + kc
                    if first_block:
                        pe.wait_ge(s_hl, c + 1)
                        if k % 2 == 0:
                            sum_h(c, first and k == 0, last and k == 2)
                    products(b, c, n * PI + k, k, first and k == 0, last and k == PI - 1, first_block)
                    if k % 2 == 0 and not (last_block and last):
                        transpose_mask(n + 1, kc, True)
                    if k == 0 and first and not first_block and not last_block:
                        lay_out_r(b + 1)
            run(pe, iteration)


_INS = ['x', 'adj', 'L0_gnn_a']


def kernel(**inputs):
    import numpy as _np
    import concourse.bacc as _bacc
    from concourse import mybir as _mybir
    from concourse.bass_utils import run_bass_kernel_spmd as _run

    nc = _bacc.Bacc("TRN2", target_bir_lowering=False, num_devices=1)
    arrays, args = {}, []
    for name in _INS:
        v = _np.ascontiguousarray(inputs[name])
        arrays[f"in_{name}_dram"] = v
        args.append(nc.dram_tensor(f"in_{name}_dram", v.shape, _mybir.dt.from_np(v.dtype), kind="ExternalInput").ap())
    shape = inputs["x"].shape
    args.append(nc.dram_tensor("out_dram", shape, _mybir.dt.from_np(_np.dtype("float32")), kind="ExternalOutput").ap())
    masked_graph_attention(nc, *args)
    r = _run(nc, [arrays], core_ids=[0])
    return r.results[0]["out_dram"]
```
